# Optimizing a Trainium2 kernel written in Bass

```python
import numpy as np
import jax
import jax.numpy as jnp

def _softmax(x, axis=-1):
    return jax.nn.softmax(x, axis=axis)

def _gelu(x):
    return jax.nn.gelu(x, approximate=True)

def _silu(x):
    return jax.nn.silu(x)

def _sigmoid(x):
    return jax.nn.sigmoid(x)

def _layernorm(x, axis=-1, eps=1e-05):
    m = jnp.mean(x, axis=axis, keepdims=True)
    v = jnp.var(x, axis=axis, keepdims=True)
    return (x - m) / jnp.sqrt(v + eps)

def _scatter_add(tgt, idx, src, axis=0):
    return tgt.at[idx].add(src)

def _segment_sum(src, seg, n):
    return jax.ops.segment_sum(src, seg, n)
kernel_name = 'mk_adj_resnorm_d2_adj_r2_2effc1'

def setup_inputs(seed: int=0):
    np.random.seed(seed)
    _w = jnp.asarray

    def _rec_inputs():
        import jax
        import jax.numpy as jnp
        _gk = jax.random.key(seed)
        x = -0.000929 + 1 * jax.random.normal(jax.random.fold_in(_gk, 1), (8192, 64), jnp.float32)
        _w = (1.0 + jnp.arange(8192, dtype=jnp.float32)) ** (-0.5)
        _w = _w / _w.mean()
        _pij = jnp.clip(0.00195312 * _w[:, None] * _w[None, :], 0.0, 1.0)
        _a = jax.random.uniform(jax.random.fold_in(_gk, 2), (8192, 8192)) < _pij
        _a = jnp.logical_or(_a, jnp.eye(8192, dtype=bool))
        _af = _a.astype(jnp.float32)
        _af = _af * jax.random.uniform(jax.random.fold_in(_gk, 3), (8192, 8192), jnp.float32, 0.05, 1)
        adj = _af
        return (x, adj)
    x, adj = _rec_inputs()

    def _L0_gnn_setup():
        import jax, jax.numpy as jnp
        import numpy as np
        P_DROP = 0.1
        key = jax.random.key(seed)
        k1, k2, k3 = jax.random.split(key, 3)
        N, D = (8192, 64)
        x = jax.random.normal(k1, (N, D), dtype=jnp.float32)
        adj = jax.random.uniform(k2, (N, N), dtype=jnp.float32)
        u = jax.random.uniform(k3, (N, D), dtype=jnp.float32)
        return {'x': x, 'adj': adj, 'u': u}
    _L0_gnn_all = _L0_gnn_setup()
    _L0_gnn_in = {k: v for k, v in _L0_gnn_all.items() if k in ('u',)}
    del _L0_gnn_all

    def _L1_gnn_setup():
        import jax, jax.numpy as jnp
        import numpy as np
        N, D_IN, D_OUT = (8192, 64, 64)
        AVG_DEG = 32.0
        L2_EPS = 1e-12
        key = jax.random.key(seed)
        kx, ka, kw, kb = jax.random.split(key, 4)
        X = jax.random.normal(kx, (N, D_IN), dtype=jnp.float32)
        adj = (jax.random.uniform(ka, (N, N)) < AVG_DEG / N).astype(jnp.float32)
        bound = 1.0 / np.sqrt(2 * D_IN)
        W = jax.random.uniform(kw, (2 * D_IN, D_OUT), dtype=jnp.float32, minval=-bound, maxval=bound)
        b = jax.random.uniform(kb, (D_OUT,), dtype=jnp.float32, minval=-bound, maxval=bound)
        return {'X': X, 'adj': adj, 'W': W, 'b': b}
    _L1_gnn_all = _L1_gnn_setup()
    _L1_gnn_in = {k: v for k, v in _L1_gnn_all.items() if k in ('W', 'b')}
    del _L1_gnn_all
    return {'x': x, 'adj': adj, 'L0_gnn_u': _L0_gnn_in['u'], 'L1_gnn_W': _L1_gnn_in['W'], 'L1_gnn_b': _L1_gnn_in['b']}

def reference(x, adj, L0_gnn_u, L1_gnn_W, L1_gnn_b):
    import jax
    import jax.numpy as jnp

    def _L0_gnn_ref(x, adj, u):
        import jax, jax.numpy as jnp
        import numpy as np
        P_DROP = 0.1
        keep = (u >= P_DROP).astype(x.dtype)
        x_drop = x * keep / (1.0 - P_DROP)
        return jnp.matmul(adj, x_drop)

    def _L1_gnn_ref(X, adj, W, b):
        import jax, jax.numpy as jnp
        import numpy as np
        N, D_IN, D_OUT = (8192, 64, 64)
        AVG_DEG = 32.0
        L2_EPS = 1e-12
        deg = jnp.clip(jnp.sum(adj, axis=1, keepdims=True) + 1.0, 1.0, None)
        h_neigh = (adj @ X + X) / deg
        concat = jnp.concatenate([X, h_neigh], axis=1)
        z = concat @ W + b
        out = jax.nn.relu(z)
        norm = jnp.linalg.norm(out, axis=1, keepdims=True)
        return out / jnp.maximum(norm, L2_EPS)
    x = _layernorm(x + _L0_gnn_ref(x, adj, L0_gnn_u), axis=-1)
    x = _layernorm(x + _L1_gnn_ref(x, adj, L1_gnn_W, L1_gnn_b), axis=-1)
    return x

_drawn_inputs = setup_inputs


def setup_inputs(seed=0):
    import zlib

    import numpy as np

    out = dict(_drawn_inputs(seed))
    spreads = {}
    factors = {'L1_gnn_b': 3.594}
    for name, (base, spread) in spreads.items():
        noise = np.random.default_rng([zlib.crc32(name.encode()), seed]).standard_normal(out[name].shape)
        drawn = base * np.exp(spread * noise) if base else spread * noise
        out[name] = jnp.asarray(drawn.astype(out[name].dtype))
    for name, factor in factors.items():
        out[name] = (out[name] * factor).astype(out[name].dtype)
    return out
```

```python
from collections import namedtuple
from contextlib import ExitStack

import concourse.bass as bass
from concourse import mybir

N, D, P = 8192, 64, 128
BLK = 512
TPB = BLK // P
NB = N // BLK
P_DROP = 0.1
LN_EPS = 1e-5
L2_EPS = 1e-12

SLOTS = 16
BAND = 4
DEFER = 12
AHEAD = 5
KEEP = 12
EARLY = 2
CHUNKS = 4
STAGE = 4

Use = namedtuple("Use", "i j slot loads")


def cached(i, j):
    return j - i < BAND and (j < DEFER or i >= KEEP)


def spread(*lists):
    at = [((n + 0.5) / len(ls), m, x) for m, ls in enumerate(lists) for n, x in enumerate(ls)]
    return [x for _, _, x in sorted(at, key=lambda e: e[:2])]


def step_events(k):
    if k == 0:
        return [("U", j) for j in range(NB)]
    wide = [("U", j) for j in range(k + BAND, NB)]
    band = [("U", j) for j in range(k, min(k + BAND, NB))]
    low = [("L", j) for j in range(k - 1)]
    pairs = [("C", m, k - 1) for m in range((k + 1) // 2)][::-1] if k - 1 < DEFER else []
    if pairs and k % 2:
        pairs[0] = ("CU",) + pairs[0][1:] + (band.pop(0)[1],)
    free = spread(wide, low)
    head, rest = free[:AHEAD], free[AHEAD:]
    hot = [p for p in pairs if cached(2 * p[1] + 1, k - 1)]
    cold = [p for p in pairs if p not in hot]
    return head + hot[:1] + spread(rest, cold, hot[1:]) + spread(band, [("L", k - 1)])


def closing_order():
    return [NB // 2 - 2, NB // 2 - 1] + list(range(NB // 2 - 3, -1, -1))


def blocks_of(k, ev):
    if ev[0] in "UL":
        return [(k, ev[1])]
    rows = [i for i in (2 * ev[1], 2 * ev[1] + 1) if i <= ev[2]]
    return [(i, ev[2]) for i in rows] + ([(k, ev[3])] if ev[0] == "CU" else [])


def closing_groups(m):
    return [[(i, j) for i in (2 * m, 2 * m + 1) if i <= j] for j in range(max(DEFER, 2 * m), NB)]


def plan():
    groups = [blocks_of(k, ev) for k in range(NB) for ev in step_events(k)]
    groups += [g for m in closing_order() for g in closing_groups(m)]
    order = [b for g in groups for b in g]
    last = {b: n for n, b in enumerate(order)}
    free_at, sums_at, loads_in = [0] * SLOTS, [0] * SLOTS, [0] * SLOTS
    held, uses, loads, sums, met = {}, [], [], 0, set()
    for group in groups:
        begin = len(uses)
        for b in group:
            if b not in held:
                slot = min((s for s in range(SLOTS) if free_at[s] is not None and free_at[s] <= begin),
                           key=lambda s: (free_at[s], s))
                loads.append((b[0], b[1], slot, free_at[slot], sums_at[slot]))
                loads_in[slot] += 1
                free_at[slot] = None
                sums_at[slot] = 0
                held[b] = slot
            slot = held[b]
            if b not in met:
                met.add(b)
                sums += 1
                sums_at[slot] = sums
            uses.append(Use(b[0], b[1], slot, loads_in[slot]))
        for n, b in enumerate(group):
            if begin + n == last[b] or not cached(*b):
                free_at[held.pop(b)] = begin + n + 1
    return uses, loads


def graph_layers_kernel(nc: bass.Bass, x: bass.AP, adj: bass.AP, u: bass.AP, w: bass.AP, b: bass.AP, out: bass.AP):
    fp32 = mybir.dt.float32
    ALU = mybir.AluOpType
    ACT = mybir.ActivationFunctionType
    AX = mybir.AxisListType
    PAIRS = NB // 2
    PT = 2 * TPB
    CT = N // P // CHUNKS
    uses, loads = plan()
    events = [step_events(k) for k in range(NB)]
    order = closing_order()
    step_end, group_end, n = [], [], 0
    for k in range(NB):
        for ev in events[k]:
            n += len(blocks_of(k, ev))
            if ev[0] in ("C", "CU"):
                group_end.append(n)
            if ev[0] != "C":
                end = n
        step_end.append(end)
    for m in order:
        n += sum(len(g) for g in closing_groups(m))
        group_end.append(n)

    with ExitStack() as ctx:
        def sb(name, shape):
            return ctx.enter_context(nc.sbuf_tensor(name, shape, fp32))

        def sem(name):
            return ctx.enter_context(nc.semaphore(name))

        adj_slots = sb("adj_slots", [P, SLOTS, TPB, BLK])
        feats = sb("feats", [P, N // P, 2 * D])
        agg2 = sb("agg2", [P, PAIRS, BLK])
        sums = sb("sums", [P, TPB * BLK])
        sums_folded = sb("sums_folded", [P, BLK])
        agg_up = sb("agg_up", [P, BLK])
        agg_low = sb("agg_low", [D, BLK])
        work = sb("work", [P, PT, D])
        squares = sb("squares", [P, PT, D])
        result = sb("result", [P, 2, PT, D])
        stat = sb("stat", [P, 8, PT])
        rdeg = sb("rdeg", [P, N // P])
        ident = sb("ident", [P, P])
        ident_two = sb("ident_two", [P, D])
        ones = sb("ones", [P, 1])
        w_par = sb("w_par", [P, 2, 2 * D])
        bias = sb("bias", [P, D])
        psum = ctx.enter_context(nc.psum_tensor("psum", [P, 8, BLK], fp32))

        UP = [psum[:, 0, :], psum[:, 2, :]]
        LOW = [psum[:, 1, :], psum[:, 3, :]]
        COL = [psum[:, 4, :], psum[:, 5, :]]
        NAT = psum[:, 6, :]
        X1T = psum[:, 7, :]
        operands = sums[:, :].rearrange("p (q n) -> p q n", q=4)
        x_stage = adj_slots[:, SLOTS - STAGE:SLOTS - STAGE // 2].rearrange("p s t n -> p (s t n)")
        u_stage = adj_slots[:, SLOTS - STAGE // 2:].rearrange("p s t n -> p (s t n)")

        slot_loaded = [sem(f"slot_loaded{s}") for s in range(SLOTS)]
        xu_loaded = [sem(f"xu_loaded{c}") for c in range(CHUNKS)]
        const_loaded = sem("const_loaded")
        masked = sem("masked")
        xd_ready = sem("xd_ready")
        consts_made = sem("consts_made")
        block_used = sem("block_used")
        summed = sem("summed")
        folded = sem("folded")
        up_out = sem("up_out")
        low_out = sem("low_out")
        nat_done = sem("nat_done")
        nat_read = sem("nat_read")
        ln_var = sem("ln_var")
        ln_std = sem("ln_std")
        x1_ready = sem("x1_ready")
        col_out = sem("col_out")
        x1t_done = sem("x1t_done")
        x1t_out = sem("x1t_out")
        z_done = sem("z_done")
        z_read = sem("z_read")
        agg_ready = sem("agg_ready")
        sq_ready = sem("sq_ready")
        norm_ready = sem("norm_ready")
        result_ready = sem("result_ready")
        stored = [sem(f"stored{q}") for q in range(2)]
        made = sem("made")
        dve_did = sem("dve_did")

        block = ctx.enter_context(nc.Block())

        @block.sync
        def _(sp):
            def load_xu(c):
                part = slice(c * CT * D, (c + 1) * CT * D)
                sp.dma_start(x_stage[:, part], x[:, part]).then_inc(xu_loaded[c], 16)
                sp.dma_start(u_stage[:, part], u[:, part]).then_inc(xu_loaded[c], 16)

            load_xu(0)
            staged = True
            for n, (i, j, slot, used, added) in enumerate(loads):
                if staged and slot >= SLOTS - STAGE:
                    sp.wait_ge(xd_ready, 2 * CHUNKS)
                    staged = False
                if used:
                    sp.wait_ge(block_used, used)
                if added:
                    sp.wait_ge(summed, added)
                sp.dma_start(adj_slots[:, slot], adj[i, j]).then_inc(slot_loaded[slot], 16)
                if n in (2, 4, 6):
                    load_xu(n // 2)
                if n == 8:
                    for par in range(2):
                        own, agg = (1 - par) * D, par * D
                        sp.wait_ge(consts_made, 1)
                        sp.dma_start(w_par[agg:agg + D, par, 0:D], w[D:2 * D, :]).then_inc(const_loaded, 16)
                        sp.dma_start(w_par[own:own + D, par, 0:D], w[D:2 * D, :]).then_inc(const_loaded, 16)
                        sp.dma_start(w_par[own:own + D, par, D:2 * D], w[0:D, :]).then_inc(const_loaded, 16)
                    sp.dma_start(bias[:, :], b.partition_broadcast(P)).then_inc(const_loaded, 16)

        @block.gpsimd
        def _(pool):
            nc.gpsimd.memset(ident[:, :], 0.0).then_inc(made, 1)
            nc.gpsimd.memset(w_par[:, :, :], 0.0).then_inc(made, 1)
            nc.gpsimd.memset(ones[:, :], 1.0).then_inc(made, 1)
            nc.gpsimd.memset(agg2[0:D, 0, :], 0.0).then_inc(made, 1)
            pool.wait_ge(made, 4)
            nc.gpsimd.affine_select(out=ident[:, :], in_=ident[:, :], compare_op=ALU.not_equal, fill=1.0,
                                    base=0, pattern=[[-1, P]], channel_multiplier=1).then_inc(made, 1)
            pool.wait_ge(made, 5)
            nc.gpsimd.tensor_tensor(ident_two[:, :], ident[:, 0:D], ident[:, D:2 * D],
                                    ALU.add).then_inc(consts_made, 1)

        @block.scalar
        def _(act):
            for c in range(CHUNKS):
                tiles = slice(c * CT, (c + 1) * CT)
                part = slice(c * CT * D, (c + 1) * CT * D)
                act.wait_ge(masked, c + 1)
                nc.scalar.activation(feats[:, tiles, 0:D], u_stage[:, part].rearrange("p (t d) -> p t d", d=D),
                                     ACT.Copy, scale=1.0 / (1.0 - P_DROP)).then_inc(xd_ready, 1)
                nc.scalar.copy(feats[:, tiles, D:2 * D],
                               x_stage[:, part].rearrange("p (t d) -> p t d", d=D)).then_inc(xd_ready, 1)

            for k in range(NB):
                act.wait_ge(block_used, step_end[k])
                if k >= 1:
                    act.wait_ge(nat_done, k)
                nc.scalar.copy(agg_up[:, :], UP[k % 2]).then_inc(up_out, 1)
                if k >= 1:
                    nc.scalar.copy(agg_low[:, :], LOW[k % 2][0:D, :]).then_inc(low_out, 1)
                    half = (k % 2) * D
                    nc.scalar.copy(agg2[half:half + D, k // 2, :], LOW[k % 2][D:2 * D, :]).then_inc(low_out, 1)
                act.wait_ge(ln_var, k + 1)
                nc.scalar.activation(stat[:, 3, 0:TPB], stat[:, 2, 0:TPB], ACT.Sqrt).then_inc(ln_std, 1)

            def finish(q):
                act.wait_ge(sq_ready, 2 * q + 1)
                nc.scalar.activation(stat[:, 1, :], stat[:, 0, :], ACT.Sqrt).then_inc(norm_ready, 1)
                act.wait_ge(sq_ready, 2 * q + 2)
                nc.scalar.activation(stat[:, 5, :], stat[:, 4, :], ACT.Sqrt).then_inc(norm_ready, 1)
                act.wait_ge(result_ready, q + 1)
                act.dma_start(out[:, order[q] * PT * D:(order[q] + 1) * PT * D],
                              result[:, q % 2].rearrange("p t d -> p (t d)")).then_inc(stored[q % 2], 16)

            for q, m in enumerate(order):
                act.wait_ge(x1t_done, q + 1)
                act.wait_ge(folded, NB)
                if q >= 2:
                    act.wait_ge(z_done, q - 1)
                nc.scalar.copy(operands[D:2 * D, 2 * (q % 2), :], X1T[D:2 * D, :]).then_inc(x1t_out, 1)
                nc.scalar.copy(operands[0:D, 2 * (q % 2) + 1, :], X1T[0:D, :]).then_inc(x1t_out, 1)
                if q >= 1:
                    finish(q - 1)
            finish(PAIRS - 1)
            for q in range(2):
                act.wait_ge(stored[q], 16 * (PAIRS // 2))

        @block.vector
        def _(dve):
            did = [0]

            def then(ins):
                did[0] += 1
                ins.then_inc(dve_did, 1)
                dve.wait_ge(dve_did, did[0])

            def wide(a, t):
                return a.unsqueeze(2).to_broadcast([P, t, D])

            for c in range(CHUNKS):
                part = slice(c * CT * D, (c + 1) * CT * D)
                dve.wait_ge(xu_loaded[c], 32)
                nc.vector.scalar_tensor_tensor(out=u_stage[:, part], in0=u_stage[:, part], scalar=P_DROP,
                                               in1=x_stage[:, part], op0=ALU.is_ge,
                                               op1=ALU.mult).then_inc(masked, 1)

            use = iter(uses)
            added = [0]
            grouped = [0]

            def add_rows(v, first):
                dve.wait_ge(slot_loaded[v.slot], 16 * v.loads)
                blk = adj_slots[:, v.slot].rearrange("p t n -> p (t n)")
                if added[0]:
                    dve.wait_ge(summed, added[0])
                if first and added[0]:
                    dve.wait_ge(folded, v.i)
                added[0] += 1
                if first:
                    nc.vector.tensor_copy(sums[:, :], blk).then_inc(summed, 1)
                else:
                    nc.vector.tensor_tensor(sums[:, :], sums[:, :], blk, ALU.add).then_inc(summed, 1)

            def fold_rows(k):
                dve.wait_ge(summed, added[0])
                then(nc.vector.tensor_tensor(sums[:, 0:2 * BLK], sums[:, 0:2 * BLK], sums[:, 2 * BLK:], ALU.add))
                if k >= 1:
                    dve.wait_ge(nat_done, k)
                nc.vector.tensor_tensor(sums_folded[:, :], sums[:, 0:BLK], sums[:, BLK:2 * BLK],
                                        ALU.add).then_inc(folded, 1)

            def centre_and_square(h, sq, total, t):
                then(nc.vector.tensor_reduce(total, h, AX.X, ALU.add))
                then(nc.vector.scalar_tensor_tensor(out=h, in0=wide(total, t), scalar=-1.0 / D, in1=h,
                                                    op0=ALU.mult, op1=ALU.add))
                then(nc.vector.tensor_tensor(sq, h, h, ALU.mult))
                then(nc.vector.tensor_reduce(total, sq, AX.X, ALU.add))

            def norm_rows(k):
                tiles = slice(k * TPB, (k + 1) * TPB)
                h = work[:, 0:TPB, :]
                agg = NAT[:, 0:TPB * D].rearrange("p (t d) -> p t d", d=D)
                dve.wait_ge(nat_done, k + 1)
                dve.wait_ge(xd_ready, 2 * CHUNKS)
                if k >= 1:
                    dve.wait_ge(x1_ready, k)
                then(nc.vector.tensor_tensor(h, agg, feats[:, tiles, D:2 * D], ALU.add))
                then(nc.vector.tensor_scalar(rdeg[:, tiles], NAT[:, TPB * D:TPB * D + TPB], 1.0, 1.0,
                                             ALU.add, ALU.max))
                nc.vector.reciprocal(rdeg[:, tiles], rdeg[:, tiles]).then_inc(nat_read, 1)
                centre_and_square(h, squares[:, 0:TPB, :], stat[:, 0, 0:TPB], TPB)
                nc.vector.tensor_scalar(stat[:, 2, 0:TPB], stat[:, 0, 0:TPB], 1.0 / D, LN_EPS, ALU.mult,
                                        ALU.add).then_inc(ln_var, 1)
                dve.wait_ge(ln_std, k + 1)
                then(nc.vector.reciprocal(stat[:, 5, 0:TPB], stat[:, 3, 0:TPB]))
                nc.vector.tensor_tensor(feats[:, tiles, D:2 * D], h, wide(stat[:, 5, 0:TPB], TPB),
                                        ALU.mult).then_inc(x1_ready, 1)

            def add_column(m, j):
                g = grouped[0]
                top = 2 * D if 2 * m + 1 <= j else D
                row = min(j, 2 * m + 1)
                dve.wait_ge(block_used, group_end[g])
                if row >= 1:
                    dve.wait_ge(low_out, 2 * row)
                else:
                    dve.wait_ge(consts_made, 1)
                if g:
                    dve.wait_ge(col_out, g)
                nc.vector.tensor_tensor(agg2[0:top, m, :], COL[g % 2][0:top, :], agg2[0:top, m, :],
                                        ALU.add).then_inc(col_out, 1)
                grouped[0] += 1

            for k in range(NB):
                first = True
                for e, ev in enumerate(events[k]):
                    if e == EARLY and k >= 1:
                        norm_rows(k - 1)
                    if ev[0] in ("C", "CU"):
                        vs = [next(use) for _ in range(len(blocks_of(k, ev)))]
                        add_column(ev[1], ev[2])
                        if ev[0] == "CU":
                            add_rows(vs[-1], first)
                            first = False
                    else:
                        add_rows(next(use), first)
                        first = False
                fold_rows(k)
            norm_rows(NB - 1)

            def finish(q):
                m = order[q]
                tiles = slice(m * PT, (m + 1) * PT)
                z = psum[:, 2 * (q % 2):2 * (q % 2) + 2, :].rearrange("p r (c w) -> p (r c) w", w=2 * D)
                own = feats[:, tiles, D:2 * D]
                y = result[:, q % 2]
                dve.wait_ge(z_done, q + 1)
                if q >= 1:
                    dve.wait_ge(result_ready, q)
                if q >= 2:
                    dve.wait_ge(stored[q % 2], 16 * (q // 2))
                then(nc.vector.tensor_tensor(work[:, :, :], z[:, :, 0:D], wide(rdeg[:, tiles], PT), ALU.mult))
                nc.vector.tensor_tensor(work[:, :, :], z[:, :, D:2 * D], work[:, :, :], ALU.add).then_inc(z_read, 1)
                dve.wait_ge(z_read, q + 1)
                then(nc.vector.tensor_tensor(work[:, :, :], work[:, :, :],
                                             bias[:, :].unsqueeze(1).to_broadcast([P, PT, D]), ALU.add))
                then(nc.vector.scalar_tensor_tensor(out=squares[:, :, :], in0=work[:, :, :], scalar=0.0,
                                                    in1=work[:, :, :], op0=ALU.max, op1=ALU.mult))
                then(nc.vector.tensor_reduce(stat[:, 0, :], squares[:, :, :], AX.X, ALU.add))
                nc.vector.tensor_scalar(stat[:, 0, :], stat[:, 0, :], L2_EPS * L2_EPS, None,
                                        ALU.max).then_inc(sq_ready, 1)
                dve.wait_ge(norm_ready, 2 * q + 1)
                then(nc.vector.reciprocal(stat[:, 2, :], stat[:, 1, :]))
                then(nc.vector.scalar_tensor_tensor(out=work[:, :, :], in0=work[:, :, :], scalar=0.0,
                                                    in1=wide(stat[:, 2, :], PT), op0=ALU.max, op1=ALU.mult))
                then(nc.vector.tensor_tensor(work[:, :, :], work[:, :, :], own, ALU.add))
                centre_and_square(work[:, :, :], squares[:, :, :], stat[:, 3, :], PT)
                nc.vector.tensor_scalar(stat[:, 4, :], stat[:, 3, :], 1.0 / D, LN_EPS, ALU.mult,
                                        ALU.add).then_inc(sq_ready, 1)
                dve.wait_ge(norm_ready, 2 * q + 2)
                then(nc.vector.reciprocal(stat[:, 6, :], stat[:, 5, :]))
                nc.vector.tensor_tensor(y, work[:, :, :], wide(stat[:, 6, :], PT),
                                        ALU.mult).then_inc(result_ready, 1)

            grouped_in_steps = grouped[0]
            dve.wait_ge(x1_ready, NB)
            dve.wait_ge(const_loaded, 7 * 16)
            for q, m in enumerate(order):
                g = grouped[0]
                dve.wait_ge(block_used, group_end[g])
                dve.wait_ge(col_out, grouped_in_steps)
                dve.wait_ge(low_out, 2 * (NB - 1))
                if q >= 2:
                    dve.wait_ge(z_done, q - 1)
                a, bb = 2 * (q % 2), 2 * (q % 2) + 1
                nc.vector.tensor_tensor(operands[0:D, a, :], COL[g % 2][0:D, :], agg2[0:D, m, :],
                                        ALU.add).then_inc(agg_ready, 1)
                nc.vector.tensor_tensor(operands[D:2 * D, bb, :], COL[g % 2][D:2 * D, :], agg2[D:2 * D, m, :],
                                        ALU.add).then_inc(agg_ready, 1)
                grouped[0] += 1
                if q >= 1:
                    finish(q - 1)
            finish(PAIRS - 1)

        @block.tensor
        def _(pe):
            use = iter(uses)
            grouped = [0]

            def arrived(v):
                pe.wait_ge(slot_loaded[v.slot], 16 * v.loads)
                return adj_slots[:, v.slot]

            def up(k, v, halves, seen, todo):
                blk = arrived(v)
                if v.i == 0 and v.j % (NB // CHUNKS) == 0:
                    pe.wait_ge(xd_ready, 2 * (v.j // (NB // CHUNKS)) + 2)
                for t, h in enumerate(halves):
                    todo[h] -= 1
                    yield nc.tensor.matmul(UP[k % 2][h * D:(h + 1) * D, :], feats[:, v.j * TPB + t, 0:D],
                                           blk[:, t, :], start=not seen[h], stop=not todo[h])
                    seen[h] = True

            def column(bank, v, seen, last):
                blk = arrived(v)
                h = v.i % 2
                for t in range(TPB):
                    yield nc.tensor.matmul(bank[h * D:(h + 1) * D, :], feats[:, v.j * TPB + t, D:2 * D],
                                           blk[:, t, :], start=not seen[h], stop=last and t == TPB - 1)
                    seen[h] = True

            def turn_back(k):
                pe.wait_ge(up_out, k + 1)
                if k >= 1:
                    pe.wait_ge(low_out, 2 * k)
                    pe.wait_ge(nat_read, k)
                else:
                    pe.wait_ge(consts_made, 1)
                for c in range(TPB):
                    cols = slice(c * P, (c + 1) * P)
                    nc.tensor.matmul(NAT[:, c * D:(c + 1) * D], agg_up[:, cols], ident_two[:, :],
                                     start=True, stop=k == 0)
                    if k >= 1:
                        nc.tensor.matmul(NAT[:, c * D:(c + 1) * D], agg_low[:, cols], ident[0:D, 0:D],
                                         start=False, stop=True)
                pe.wait_ge(folded, k + 1)
                for c in range(TPB):
                    done = nc.tensor.matmul(NAT[:, TPB * D + c:TPB * D + c + 1], sums_folded[:, c * P:(c + 1) * P],
                                            ones[:, :], start=True, stop=True)
                done.then_inc(nat_done, 1)

            for k in range(NB):
                if k >= 2:
                    pe.wait_ge(up_out, k - 1)
                    if k >= 3:
                        pe.wait_ge(low_out, 2 * (k - 2))
                seen = [False, False]
                todo = [0, 0]
                for ev in events[k]:
                    for h in ((0, 1, 0, 1) if ev[0] == "U" else (1, 1, 1, 1) if ev[0] == "CU" else ()):
                        todo[h] += 1
                assert min(todo) > 0
                lows, lows_todo = 0, TPB * k
                for e, ev in enumerate(events[k]):
                    if e == EARLY and k >= 1:
                        turn_back(k - 1)
                    if ev[0] == "U":
                        for done in up(k, next(use), (0, 1, 0, 1), seen, todo):
                            pass
                        done.then_inc(block_used, 1)
                    elif ev[0] == "L":
                        v = next(use)
                        blk = arrived(v)
                        pe.wait_ge(x1_ready, v.j + 1)
                        for t in range(TPB):
                            done = nc.tensor.matmul(LOW[k % 2], feats[:, v.j * TPB + t, :], blk[:, t, :],
                                                    start=not lows, stop=lows == lows_todo - 1)
                            lows += 1
                        done.then_inc(block_used, 1)
                    else:
                        g = grouped[0]
                        vs = [next(use) for _ in range(len(blocks_of(k, ev)))]
                        pe.wait_ge(x1_ready, ev[2] + 1)
                        if g >= 2:
                            pe.wait_ge(col_out, g - 1)
                        fresh = [False, False]
                        one = column(COL[g % 2], vs[0], fresh, True)
                        two = (up(k, vs[1], (1, 1, 1, 1), seen, todo) if ev[0] == "CU"
                               else column(COL[g % 2], vs[1], fresh, True))
                        for done_one, done in zip(one, two):
                            pass
                        done_one.then_inc(block_used, 1)
                        done.then_inc(block_used, 1)
                        grouped[0] += 1

            def turn_x1(q):
                m = order[q]
                pe.wait_ge(x1_ready, 2 * m + 2)
                if q >= 1:
                    pe.wait_ge(x1t_out, 2 * q)
                for c in range(TPB):
                    for par in range(2):
                        half = (1 - par) * D
                        done = nc.tensor.matmul(X1T[half:half + D, c * P:(c + 1) * P],
                                                feats[:, (2 * m + par) * TPB + c, D:2 * D], ident[:, :],
                                                start=True, stop=True)
                done.then_inc(x1t_done, 1)

            def times_w(q):
                pe.wait_ge(agg_ready, 2 * q + 2)
                pe.wait_ge(x1t_out, 2 * q + 2)
                if q >= 2:
                    pe.wait_ge(z_read, q - 1)
                for par in range(2):
                    for c in range(TPB):
                        done = nc.tensor.matmul(psum[:, 2 * (q % 2) + par, c * P:(c + 1) * P],
                                                operands[:, 2 * (q % 2) + par, c * P:(c + 1) * P],
                                                w_par[:, par, :], start=True, stop=True)
                done.then_inc(z_done, 1)

            pe.wait_ge(const_loaded, 7 * 16)
            in_steps = grouped[0]
            for q, m in enumerate(order):
                turn_x1(q)
                g = grouped[0]
                if q >= 2:
                    pe.wait_ge(agg_ready, 2 * (q - 1))
                else:
                    pe.wait_ge(col_out, in_steps - 1 + q)
                fresh = [False, False]
                ended = 0
                for pair in closing_groups(m):
                    j = pair[0][1]
                    vs = [next(use) for _ in pair]
                    pe.wait_ge(x1_ready, j + 1)
                    runs = [column(COL[g % 2], v, fresh, j == NB - 1) for v in vs]
                    for dones in zip(*runs):
                        pass
                    for done in dones:
                        done.then_inc(block_used, 1)
                    if ended < 2 <= ended + len(pair):
                        if q == 0:
                            turn_back(NB - 1)
                        else:
                            times_w(q - 1)
                    ended += len(pair)
                grouped[0] += 1
            times_w(PAIRS - 1)


def kernel(x, adj, L0_gnn_u, L1_gnn_W, L1_gnn_b):
    import numpy as np
    import concourse.bacc as bacc
    from concourse.bass_utils import run_bass_kernel_spmd

    def by_tiles(a):
        return np.ascontiguousarray(np.asarray(a).reshape(N // P, P, D).transpose(1, 0, 2)).reshape(P, -1)

    nc = bacc.Bacc("TRN2", target_bir_lowering=False, num_devices=1)
    arrays = {
        "x": by_tiles(x),
        "adj": np.ascontiguousarray(
            np.asarray(adj).reshape(NB, BLK, NB, TPB, P).transpose(0, 2, 4, 3, 1)),
        "u": by_tiles(L0_gnn_u),
        "w": np.ascontiguousarray(L1_gnn_W),
        "b": np.ascontiguousarray(L1_gnn_b),
    }
    args = [nc.dram_tensor(f"in_{name}", a.shape, mybir.dt.float32, kind="ExternalInput").ap()
            for name, a in arrays.items()]
    out = nc.dram_tensor("out", (P, N // P * D), mybir.dt.float32, kind="ExternalOutput").ap()
    graph_layers_kernel(nc, *args, out)
    r = run_bass_kernel_spmd(nc, [{f"in_{name}": a for name, a in arrays.items()}], core_ids=[0])
    got = r.results[0]["out"]
    return np.ascontiguousarray(got.reshape(P, N // P, D).transpose(1, 0, 2)).reshape(N, D)
```
